# Optimizing a Trainium2 kernel written in Bass

```python
import numpy as np
import jax
import jax.numpy as jnp

def _softmax(x, axis=-1):
    return jax.nn.softmax(x, axis=axis)

def _gelu(x):
    return jax.nn.gelu(x, approximate=True)

def _silu(x):
    return jax.nn.silu(x)

def _sigmoid(x):
    return jax.nn.sigmoid(x)

def _layernorm(x, axis=-1, eps=1e-05):
    m = jnp.mean(x, axis=axis, keepdims=True)
    v = jnp.var(x, axis=axis, keepdims=True)
    return (x - m) / jnp.sqrt(v + eps)

def _scatter_add(tgt, idx, src, axis=0):
    return tgt.at[idx].add(src)

def _segment_sum(src, seg, n):
    return jax.ops.segment_sum(src, seg, n)
kernel_name = 'mk_prb_d1_jaxref_r4_e641d0'

def setup_inputs(seed: int=0):
    np.random.seed(seed)
    _w = jnp.asarray

    def _L0_attn_setup():
        import jax, jax.numpy as jnp
        import numpy as np
        B, S, H, NH = (1, 1024, 256, 16)
        DH = H // NH

        def _split_heads(x):
            b, s, h = x.shape
            return jnp.transpose(x.reshape(b, s, NH, DH), (0, 2, 1, 3))
        key = jax.random.key(seed)
        ks = jax.random.split(key, 9)
        sc = 0.02
        return {'queries': jax.random.normal(ks[0], (B, S, H), jnp.float32), 'keys': jax.random.normal(ks[1], (B, S, H), jnp.float32), 'values': jax.random.normal(ks[2], (B, S, H), jnp.float32), 'Wq_w': jax.random.normal(ks[3], (H, H), jnp.float32) * sc, 'Wq_b': jax.random.normal(ks[4], (H,), jnp.float32) * sc, 'Wk_w': jax.random.normal(ks[5], (H, H), jnp.float32) * sc, 'Wk_b': jax.random.normal(ks[6], (H,), jnp.float32) * sc, 'Wv_w': jax.random.normal(ks[7], (H, H), jnp.float32) * sc, 'Wv_b': jax.random.normal(ks[8], (H,), jnp.float32) * sc}
    _L0_attn_in = _L0_attn_setup()

    def _L0_ffn_setup():
        import jax, jax.numpy as jnp
        import numpy as np
        MAX_VAL = 100.0
        key = jax.random.key(seed)
        k1, k2, k3 = jax.random.split(key, 3)
        B, S, D_IN, D_OUT = (4, 2048, 256, 256)
        x = jax.random.normal(k1, (B, S, D_IN), dtype=jnp.float32)
        weights = jax.random.normal(k2, (D_OUT, D_IN), dtype=jnp.float32)
        scale = jnp.ones((D_OUT,), dtype=jnp.float32)
        bias = jax.random.normal(k3, (D_OUT,), dtype=jnp.float32)
        return {'x': x, 'weights': weights, 'scale': scale, 'bias': bias}
    _L0_ffn_in = _L0_ffn_setup()
    _d = {'L0_attn_queries': _L0_attn_in['queries'], 'L0_attn_keys': _L0_attn_in['keys'], 'L0_attn_values': _L0_attn_in['values'], 'L0_attn_Wq_w': _L0_attn_in['Wq_w'], 'L0_attn_Wq_b': _L0_attn_in['Wq_b'], 'L0_attn_Wk_w': _L0_attn_in['Wk_w'], 'L0_attn_Wk_b': _L0_attn_in['Wk_b'], 'L0_attn_Wv_w': _L0_attn_in['Wv_w'], 'L0_attn_Wv_b': _L0_attn_in['Wv_b'], 'L0_ffn_weights': _L0_ffn_in['weights'], 'L0_ffn_scale': _L0_ffn_in['scale'], 'L0_ffn_bias': _L0_ffn_in['bias']}
    _x0 = _d['L0_attn_queries']
    _d['L0_attn_queries'] = jax.random.normal(jax.random.fold_in(jax.random.key(seed), 1), (16, 1024, 256), dtype=_x0.dtype)
    del _x0
    return _d

def reference(L0_attn_queries, L0_attn_keys, L0_attn_values, L0_attn_Wq_w, L0_attn_Wq_b, L0_attn_Wk_w, L0_attn_Wk_b, L0_attn_Wv_w, L0_attn_Wv_b, L0_ffn_weights, L0_ffn_scale, L0_ffn_bias):

    def _L0_attn_ref(queries, keys, values, Wq_w, Wq_b, Wk_w, Wk_b, Wv_w, Wv_b):
        import jax, jax.numpy as jnp
        import numpy as np
        B, S, H, NH = (1, 1024, 256, 16)
        DH = H // NH

        def _split_heads(x):
            b, s, h = x.shape
            return jnp.transpose(x.reshape(b, s, NH, DH), (0, 2, 1, 3))
        q = jax.nn.relu(queries @ Wq_w.T + Wq_b)
        k = jax.nn.relu(keys @ Wk_w.T + Wk_b)
        v = jax.nn.relu(values @ Wv_w.T + Wv_b)
        qh, kh, vh = (_split_heads(q), _split_heads(k), _split_heads(v))
        score = jnp.einsum('bhsd,bhtd->bhst', qh, kh) / jnp.sqrt(jnp.float32(DH))
        attn = jax.nn.softmax(score, axis=-1)
        a = jnp.einsum('bhst,bhtd->bhsd', attn, vh)
        a = jnp.transpose(a, (0, 1, 3, 2)).reshape(q.shape[0], q.shape[1], q.shape[2])
        return a + queries

    def _L0_ffn_ref(x, weights, scale, bias):
        import jax, jax.numpy as jnp
        import numpy as np
        MAX_VAL = 100.0
        w = (weights >= 0.0).astype(x.dtype) * 2.0 - 1.0
        y = jnp.einsum('bsi,oi->bso', x, w)
        y = y * scale + bias
        y = jnp.clip(y, -MAX_VAL, MAX_VAL)
        return y
    x = L0_attn_queries
    xn = _layernorm(x, axis=-1)
    x = x + _L0_attn_ref(xn, L0_attn_keys, L0_attn_values, L0_attn_Wq_w, L0_attn_Wq_b, L0_attn_Wk_w, L0_attn_Wk_b, L0_attn_Wv_w, L0_attn_Wv_b) + _L0_ffn_ref(xn, L0_ffn_weights, L0_ffn_scale, L0_ffn_bias)
    return x

_drawn_inputs = setup_inputs


def setup_inputs(seed=0):
    import zlib

    import numpy as np

    out = dict(_drawn_inputs(seed))
    spreads = {'L0_ffn_scale': (1.0, 0.2)}
    factors = {'L0_attn_keys': 8.0,
     'L0_attn_values': 8.0,
     'L0_attn_Wq_w': 8.0,
     'L0_attn_Wq_b': 8.0,
     'L0_attn_Wk_w': 8.0,
     'L0_attn_Wk_b': 55.889,
     'L0_attn_Wv_w': 8.0,
     'L0_attn_Wv_b': 64.0}
    for name, (base, spread) in spreads.items():
        noise = np.random.default_rng([zlib.crc32(name.encode()), seed]).standard_normal(out[name].shape)
        drawn = base * np.exp(spread * noise) if base else spread * noise
        out[name] = jnp.asarray(drawn.astype(out[name].dtype))
    for name, factor in factors.items():
        out[name] = (out[name] * factor).astype(out[name].dtype)
    return out
```

```python
from contextlib import ExitStack

import concourse.bass as bass
from concourse import mybir

FP32 = mybir.dt.float32
BF16 = mybir.dt.bfloat16
ALU = mybir.AluOpType
ACT = mybir.ActivationFunctionType
AX = mybir.AxisListType


def attention_block(nc: bass.Bass, x, keys_t, values_t, wq_t, bq, wk_t, bk, wv_t, bv, wf_t, scale, bias, out):
    P = 128
    NB, S, H = x.shape
    T = keys_t.shape[1]
    NH = 16
    DH = H // NH
    EPS = 1e-5
    LIMIT = 100.0
    BANK = 512
    IC = H // P
    HALF = NH // 2
    GROUP = 4
    J = H * 4 // S * 4
    NST = S // P
    NTH = T // BANK
    NTC = T // P
    NA = S // BANK
    TERMS = (0, 0, 1, 0, 2, 1)
    KTERMS = (0, 1, 0, 2, 0, 1)
    KS = len(TERMS) * DH
    KM = KS + 3
    QUADS = HALF // GROUP * NA * (NTC // 2)
    UNITS = QUADS * GROUP
    TILES = HALF * NST * NTH
    PER_QUAD = 10
    EXP_SCALE = float(DH) ** -0.5

    ctx = ExitStack()
    with ctx:
        def sb(name, shape, dt):
            return ctx.enter_context(nc.sbuf_tensor(name, shape, dt))

        def sem(name):
            return ctx.enter_context(nc.semaphore(name))

        kstack = sb("kstack", [KM, NH, T], BF16)
        qstack = [sb(f"qstack{i}", [KM, HALF, S], BF16) for i in range(2)]
        vones = sb("vones", [P, NTC, NH, DH, 2], FP32)
        probs = sb("probs", [P, 2 * GROUP, 2 * BANK], FP32)
        parts = sb("parts", [P, 3, 2, S], BF16)
        proj = sb("proj", [P, 2, BANK], FP32)
        mrows = proj[0:3 * HALF, 0, :].bitcast(BF16)
        xin = sb("xin", [P, NA, J, H], FP32)
        xn = sb("xn", [P, NA, J, H], FP32)
        xnT = sb("xnT", [P, IC, BANK], FP32)
        dense = sb("dense", [P, NA, 2, BANK], FP32)
        base_new = sb("base_new", [P, NA, J * H], FP32)
        base_cur = sb("base_cur", [P, NA, J * H], FP32)
        taken = sb("taken", [P, 2, BANK], FP32)
        fin = sb("fin", [P, 2, S], FP32)
        wq_sb = sb("wq_sb", [P, IC, H], FP32)
        wf_sb = sb("wf_sb", [P, IC, H], FP32)
        bias_row = sb("bias_row", [1, H], FP32)
        ident = sb("ident", [P, P], FP32)
        identb = sb("identb", [P, P], BF16)
        mx = sb("mx", [P, NST, HALF, NTH], FP32)
        mneg = sb("mneg", [P, NST, HALF], FP32)
        mrest = sb("mrest", [P, NST, HALF], FP32)
        mparts = sb("mparts", [P, NST, 3, HALF], BF16)
        stats = sb("stats", [P, NA, J, 6], FP32)
        meanvar = sb("meanvar", [P, NA, J, 2], FP32)
        rstd = sb("rstd", [P, NA, J], FP32)
        shift = sb("shift", [P, NA, J], FP32)
        newton = sb("newton", [P, J], FP32)
        varp = sb("varp", [P, J], FP32)
        const = sb("const", [P, 5], FP32)
        bq_sb = sb("bq_sb", [P, 2], FP32)
        bk_sb = sb("bk_sb", [P, 2], FP32)
        C_EPS, C_MHALF, C_3HALF, C_MONE, C_ONE = (const[:, i:i + 1] for i in range(5))
        ones_row = vones[0:1, 0, 0:HALF, :, 1]

        keys_sb = probs[:, 0:2, :]
        vals_sb = probs[:, 2:4, :]
        wk_sb = probs[:, 4, 0:BANK].rearrange("p (c o) -> p c o", c=IC)
        wv_sb = probs[:, 4, BANK:2 * BANK].rearrange("p (c o) -> p c o", c=IC)
        wft_sb = probs[:, 5, 0:BANK].rearrange("p (c o) -> p c o", c=IC)
        sign_sb = probs[:, 5, BANK:2 * BANK].rearrange("p (c o) -> p c o", c=IC)
        scale_row = probs[0:1, 6, 0:H]
        bv_row = probs[0:1, 6, H:2 * H]

        score_ps = [ctx.enter_context(nc.psum_tensor(f"score_ps{i}", [P, 2 * BANK], FP32)) for i in range(2)]
        value_ps = ctx.enter_context(nc.psum_tensor("value_ps", [P, BANK], FP32))
        RING = 3
        ring = [ctx.enter_context(nc.psum_tensor(f"ring{i}", [P, BANK], FP32)) for i in range(RING)]

        s_id = sem("s_id")
        s_ones = sem("s_ones")
        s_wk = sem("s_wk")
        s_wv = sem("s_wv")
        s_wf = sem("s_wf")
        s_wq = sem("s_wq")
        s_kp = sem("s_kp")
        s_kr = sem("s_kr")
        s_kc = sem("s_kc")
        s_ks = sem("s_ks")
        s_kd = sem("s_kd")
        s_vp = sem("s_vp")
        s_vr = sem("s_vr")
        s_sc = sem("s_sc")
        s_sg = sem("s_sg")
        s_ws = sem("s_ws")
        s_xin = sem("s_xin")
        s_stats = sem("s_stats")
        s_mv = sem("s_mv")
        s_rc = sem("s_rc")
        s_rstd = sem("s_rstd")
        s_xn = sem("s_xn")
        s_xT = sem("s_xT")
        s_xTc = sem("s_xTc")
        s_q = sem("s_q")
        s_qr = sem("s_qr")
        s_qc = sem("s_qc")
        s_split = sem("s_split")
        s_load = [[sem(f"s_load{i}{g}") for g in range(2)] for i in range(2)]
        s_f = sem("s_f")
        s_dense = sem("s_dense")
        s_base = sem("s_base")
        s_badd = sem("s_badd")
        s_bcopy = sem("s_bcopy")
        s_mm = sem("s_mm")
        s_mx = sem("s_mx")
        s_mc = sem("s_mc")
        s_ms = sem("s_ms")
        s_mT = sem("s_mT")
        s_mrow = sem("s_mrow")
        s_rows = [sem(f"s_rows{i}") for i in range(2)]
        s_scores = sem("s_scores")
        s_probs = sem("s_probs")
        s_pv = sem("s_pv")
        s_taken = sem("s_taken")
        s_gather = [sem(f"s_gather{i}") for i in range(2)]
        s_rec = sem("s_rec")
        s_norm = sem("s_norm")
        s_res = sem("s_res")
        s_out = sem("s_out")

        def wait(eng, s, value):
            if not (isinstance(value, int) and value <= 0):
                eng.wait_ge(s, value)

        def quad_of(q):
            return q // (NA * NTC // 2), q // (NTC // 2) % NA, q % (NTC // 2)

        def ring_order(jobs):
            return [(*job, n % RING) for n, job in enumerate(jobs)]

        AHEAD = [(kind, a, i) for a in range(NA) for kind in ("turn", "project", "dense") for i in range(2)]
        AHEAD_QUADS = {("turn", 0): 3, ("project", 0): 4, ("dense", 0): 5,
                       ("turn", 1): 6, ("project", 1): 7, ("dense", 1): 8}
        ROWS_QUAD = 14
        SETUP = [("keys", n) for n in range(2 * NTH)] + [("scale", 0)] + [("values", n) for n in range(NTC // 2)]
        SETUP_BANKS = {job: n % RING for n, job in enumerate(SETUP)}
        assert len(SETUP) % RING == 0 and len(AHEAD) % RING == 0

        def ring_jobs(ahead):
            steps, n, order = [], 0, 0
            for q in range(QUADS):
                for u in range(GROUP):
                    jobs = []
                    for _ in range((3, 2, 3, 2)[u]):
                        if n < TILES:
                            jobs.append(("max", n, 0))
                            n += 1
                    if u == 2 and ahead:
                        jobs += [job for job in AHEAD if AHEAD_QUADS[job[:2]] == q]
                    if u == 3 and q == ROWS_QUAD:
                        jobs.append(("rows", 0, 0))
                    steps.append([(*job, (order + i) % RING) for i, job in enumerate(jobs)])
                    order += len(jobs)
            assert n == TILES and order % RING == 0
            return steps

        def run(eng, half_step):
            half_step(0, 0, None, None, False)
            half_step(0, 1, (0, 0), None, True)
            with eng.Fori(1, NB - 1) as b:
                half_step(b, 0, (b - 1, 1), (b - 1, 0), False)
                half_step(b, 1, (b, 0), (b - 1, 1), True)
            half_step(NB - 1, 0, (NB - 2, 1), (NB - 2, 0), False)
            half_step(NB - 1, 1, (NB - 1, 0), (NB - 2, 1), False)
            half_step(None, None, (NB - 1, 1), (NB - 1, 0), False)
            half_step(None, None, None, (NB - 1, 1), False)

        block = ctx.enter_context(nc.Block())

        @block.sync
        def _(sp):
            def load_x(b):
                sp.dma_start(xin[:, :, :, :], x[b].rearrange("(a p j) c -> p a j c", p=P, j=J)).then_inc(s_xin, 16)

            def stack(dst, head, chunk, g, terms, s):
                for r, term in enumerate(terms):
                    sp.dma_start(dst[r * DH:(r + 1) * DH, head:head + GROUP, :],
                                 parts[g * GROUP * DH:(g + 1) * GROUP * DH, term, chunk, :]).then_inc(s, 16)

            def fixed(value):
                return value if isinstance(value, int) else sp.to_reg(value)

            def load_queries(b, hh, g):
                stack(qstack[hh], g * GROUP, hh, g, TERMS, s_load[hh][g])

            def gather(b, hh, a):
                before, now = fixed((b * 2 + hh) * 16), fixed(b * 8 + hh * 4 + a + 1)
                if a == 0:
                    wait(sp, s_out, before)
                sp.wait_ge(s_taken, now)
                g = a // NA
                sp.dma_start(fin[g * 64:(g + 1) * 64, :, (a % NA) * BANK:(a % NA + 1) * BANK],
                             taken[:, a % 2, :]).then_inc(s_gather[a % 2], 16)

            load_x(0)
            sp.dma_start(keys_sb, keys_t.rearrange("(c p) t -> p c t", p=P)).then_inc(s_wk, 16)
            sp.dma_start(wk_sb, wk_t.rearrange("(c p) o -> p c o", p=P)).then_inc(s_wk, 16)
            sp.dma_start(bk_sb[:, :], bk).then_inc(s_wk, 16)
            sp.dma_start(wft_sb, wf_t.rearrange("(c p) o -> p c o", p=P)).then_inc(s_wf, 16)
            sp.dma_start(scale_row, scale).then_inc(s_wf, 16)
            sp.dma_start(bias_row[:, :], bias).then_inc(s_wf, 16)
            sp.dma_start(wq_sb[:, :, :], wq_t.rearrange("(c p) o -> p c o", p=P)).then_inc(s_wq, 16)
            sp.dma_start(bq_sb[:, :], bq).then_inc(s_wq, 16)
            sp.dma_start(vals_sb, values_t.rearrange("(c p) t -> p c t", p=P)).then_inc(s_wv, 16)
            sp.dma_start(wv_sb, wv_t.rearrange("(c p) o -> p c o", p=P)).then_inc(s_wv, 16)
            sp.dma_start(bv_row, bv).then_inc(s_wv, 16)
            sp.wait_ge(s_ks, NA)
            for oc in range(2):
                for g in range(2):
                    stack(kstack, oc * HALF + g * GROUP, oc, g, KTERMS, s_kd)
            sp.wait_ge(s_split, NA)
            load_queries(0, 0, 0)

            def half_step(b, hh, att, last, ahead):
                if last:
                    gather(*last, 3)
                if b is not None:
                    load_queries(b, hh, 1)
                if b is not None and hh == 0 and not (isinstance(b, int) and b == NB - 1):
                    sp.wait_ge(s_badd, b * 4 + 4)
                    load_x(b + 1)
                if last:
                    fb, fh = last
                    result = out[fb].rearrange("(f p j) c -> f p (j c)", f=2, p=P)[fh]
                    sp.wait_ge(s_res, fb * 2 + fh + 1)
                    sp.dma_start(result, fin[:, 1, :]).then_inc(s_out, 16)
                if b is not None and hh == 1:
                    sp.wait_ge(s_badd, b * 4 + 4)
                    sp.dma_start(base_cur[:, :, :], base_new[:, :, :]).then_inc(s_bcopy, 16)
                if att:
                    gather(*att, 0)
                    gather(*att, 1)
                if b is not None and hh == 0:
                    load_queries(b, 1, 0)
                if ahead:
                    sp.wait_ge(s_split, b * NA + 2 * NA)
                    load_queries(b + 1, 0, 0)
                if att:
                    gather(*att, 2)
                if b is not None:
                    sp.wait_ge(s_mrow, b * 2 + hh + 1)
                    sp.dma_start(qstack[hh][KS:KM, :, :], mrows).then_inc(s_rows[hh], 16)

            run(sp, half_step)
            sp.wait_ge(s_out, NB * 2 * 16)

        @block.tensor
        def _(pe):
            users = []

            def bank(b, n, s, per, k, shift=0):
                if len(users) >= RING:
                    s0, per0, k0, shift0 = users[-RING]
                    pe.wait_ge(s0, (b + shift0) * per0 + k0)
                assert n == len(users) % RING
                users.append((s, per, k, shift))
                return ring[n]

            def scores(b, hh, u):
                g, a, tp = quad_of(u // GROUP)
                h = g * GROUP + u % GROUP
                if u == 0:
                    pe.wait_ge(s_rows[hh], b * 16 + 16)
                wait(pe, s_probs, b * 2 * UNITS + hh * UNITS + u - 1)
                for c in range(2):
                    tc = 2 * tp + c
                    mm = pe.matmul(score_ps[u % 2][:, c * BANK:(c + 1) * BANK],
                                   kstack[0:KM, hh * HALF + h, tc * P:(tc + 1) * P],
                                   qstack[hh][0:KM, h, a * BANK:(a + 1) * BANK], start=True, stop=True)
                mm.then_inc(s_scores, 1)

            def weigh(b, hh, q, c):
                g, a, tp = quad_of(q)
                if c == 0:
                    pe.wait_ge(s_probs, b * 2 * UNITS + hh * UNITS + GROUP * (q + 1))
                    if tp == 0:
                        wait(pe, s_taken, b * 8 + hh * 4 + q // 4)
                for h4 in range(GROUP):
                    mm = pe.matmul(value_ps[h4 * 32:(h4 + 1) * 32, :],
                                   vones[:, 2 * tp + c, hh * HALF + g * GROUP + h4, :, :],
                                   probs[:, q % 2 * GROUP + h4, c * BANK:(c + 1) * BANK],
                                   start=(tp == 0 and c == 0), stop=(tp == NTC // 2 - 1 and c == 1))
                if c == 1:
                    mm.then_inc(s_pv, 1)

            def maxima(b, hh, n, to):
                h, st, th = n // (NST * NTH), n // NTH % NST, n % NTH
                if n % (TILES // 2) == 0:
                    pe.wait_ge(s_load[hh][n // (TILES // 2)], b * 16 * len(TERMS) + 16 * len(TERMS))
                ps = bank(b, to, s_mx, 2 * TILES, hh * TILES + n + 1)
                pe.matmul(ps[:, :], qstack[hh][0:KS, h, st * P:(st + 1) * P],
                          kstack[0:KS, hh * HALF + h, th * BANK:(th + 1) * BANK],
                          start=True, stop=True).then_inc(s_mm, 1)

            def turn_maxima(b, hh, to):
                ps = bank(b, to, s_mrow, 2, hh + 1)
                pe.wait_ge(s_ms, b * 2 + hh + 1)
                rows = ps[0:3 * HALF, :].bitcast(BF16)
                for st in range(NST):
                    mm = pe.transpose(rows[:, st * P:(st + 1) * P], mparts[:, st, :, :], identb[:, :])
                mm.then_inc(s_mT, 1)

            def next_batch(b, kind, a, i, to):
                if kind == "turn":
                    ps = bank(b, to, s_xTc, 4, a * 2 + i + 1, 1)
                    pe.wait_ge(s_xn, (b + 1) * NA + a + 1)
                    for j in range(J):
                        mm = pe.transpose(ps[:, j * P:(j + 1) * P], xn[:, a, j, i * P:(i + 1) * P], ident[:, :])
                    mm.then_inc(s_xT, 1)
                elif kind == "project":
                    ps = bank(b, to, s_qr, 4, a * 2 + i + 1, 1)
                    pe.wait_ge(s_xTc, (b + 1) * 4 + a * 2 + 2)
                    for ic in range(IC):
                        mm = pe.matmul(ps[:, :], wq_sb[:, ic, i * P:(i + 1) * P], xnT[:, ic, :],
                                       start=(ic == 0), stop=(ic == IC - 1))
                    mm.then_inc(s_q, 1)
                else:
                    ps = bank(b, to, s_dense, 4, a * 2 + i + 1, 1)
                    for j in range(2):
                        dst = ps[:, j * H:(j + 1) * H]
                        pe.matmul(dst, ones_row, bias_row[:, :], start=True, stop=False)
                        for ic in range(IC):
                            col = (i * 2 + j) * P
                            mm = pe.matmul(dst, xnT[:, ic, col:col + P], wf_sb[:, ic, :],
                                           start=False, stop=(ic == IC - 1))
                    mm.then_inc(s_f, 1)

            pe.wait_ge(s_id, 6)
            pe.wait_ge(s_wk, 48)
            for n in range(2 * NTH):
                a, oc = n // 2, n % 2
                ps = bank(0, SETUP_BANKS["keys", n], s_kr, 0, n + 1)
                for ic in range(IC):
                    mm = pe.matmul(ps[:, :], wk_sb[:, ic, oc * P:(oc + 1) * P],
                                   keys_sb[:, ic, a * BANK:(a + 1) * BANK],
                                   start=(ic == 0), stop=(ic == IC - 1))
                mm.then_inc(s_kp, 1)
            pe.wait_ge(s_wf, 48)
            ps = bank(0, SETUP_BANKS["scale", 0], s_ws, 0, 1)
            pe.matmul(ps[:, 0:H], ones_row, scale_row, start=True, stop=True).then_inc(s_sc, 1)
            pe.wait_ge(s_wv, 48)
            for n in range(NTC // 2):
                ps = bank(0, SETUP_BANKS["values", n], s_vr, 0, n + 1)
                for i in range(2):
                    tc = 2 * n + i
                    dst = ps[:, i * H:(i + 1) * H]
                    pe.matmul(dst, ones_row, bv_row, start=True, stop=False)
                    for ic in range(IC):
                        mm = pe.matmul(dst, vals_sb[:, ic, tc * P:(tc + 1) * P], wv_sb[:, ic, :],
                                       start=False, stop=(ic == IC - 1))
                mm.then_inc(s_vp, 1)
            pe.wait_ge(s_wq, 32)
            pe.wait_ge(s_ws, 1)
            for job in ring_order(AHEAD):
                next_batch(-1, *job)
            pe.wait_ge(s_kd, 4 * 16 * len(TERMS))
            pe.wait_ge(s_ones, 1)

            def half_step(b, hh, att, last, ahead):
                if b is not None and hh == 0:
                    users[-RING:] = [(s, per, k, shift - 1) for s, per, k, shift in users[-RING:]]
                steps = ring_jobs(ahead)
                for i in range(UNITS):
                    q, u = i // GROUP, i % GROUP
                    if att:
                        scores(*att, i)
                    if b is not None:
                        for kind, a, k, to in steps[i]:
                            if kind == "max":
                                maxima(b, hh, a, to)
                            elif kind == "rows":
                                turn_maxima(b, hh, to)
                            else:
                                next_batch(b, kind, a, k, to)
                    if u % 2 and (last if q == 0 else att):
                        weigh(*(last if q == 0 else att), (q - 1) % QUADS, u // 2)

            run(pe, half_step)

        @block.scalar
        def _(act):
            def exponentials(b, hh, u):
                q = u // GROUP
                if u % GROUP == 0:
                    wait(act, s_pv, b * 2 * QUADS + hh * QUADS + q - 1)
                act.wait_ge(s_scores, b * 2 * UNITS + hh * UNITS + u + 1)
                nc.scalar.activation(probs[:, q % 2 * GROUP + u % GROUP, :], score_ps[u % 2][:, :],
                                     ACT.Exp, scale=EXP_SCALE).then_inc(s_probs, 1)

            def take(b, hh, a):
                wait(act, s_gather[a % 2], (b * 4 + hh * 2 + a // 2) * 16)
                act.wait_ge(s_pv, b * 2 * QUADS + hh * QUADS + 4 * a + 4)
                nc.scalar.activation(taken[:, a % 2, :], value_ps[:, :], ACT.Copy).then_inc(s_taken, 1)

            def take_job(b, hh, ahead, kind, a, i, src):
                if kind == "turn":
                    if i == 0:
                        wait(act, s_f, (b + 1) * 4 + a * 2)
                    act.wait_ge(s_xT, (b + 1) * 4 + a * 2 + i + 1)
                    nc.scalar.activation(xnT[:, i, :], ring[src][:, :], ACT.Copy).then_inc(s_xTc, 1)
                if kind == "project":
                    if i == 0:
                        wait(act, s_split, (b + 1) * NA + a)
                        if a == 0:
                            wait(act, s_rows[0], (b + 1) * 16)
                            wait(act, s_rows[1], b * 16)
                    act.wait_ge(s_q, (b + 1) * 4 + a * 2 + i + 1)
                    nc.scalar.activation(proj[:, i, :], ring[src][:, :], ACT.Relu,
                                         bias=bq_sb[:, i:i + 1]).then_inc(s_qr, 1)
                if kind == "rows":
                    act.wait_ge(s_mT, b * 2 + hh + 1)
                    wait(act, s_split, (b + 2 if ahead else b + 1) * NA)
                    wait(act, s_rows[1 - hh], (b + hh) * 16)
                    nc.scalar.activation(mrows, ring[src][0:3 * HALF, :].bitcast(BF16),
                                         ACT.Copy).then_inc(s_mrow, 1)

            act.wait_ge(s_wk, 48)
            for n in range(2 * NTH):
                a, oc = n // 2, n % 2
                if n == 2:
                    act.wait_ge(s_ks, 1)
                act.wait_ge(s_kp, n + 1)
                nc.scalar.activation(proj[:, oc, :], ring[SETUP_BANKS["keys", n]][:, :], ACT.Relu,
                                     bias=bk_sb[:, oc:oc + 1]).then_inc(s_kr, 1)
            act.wait_ge(s_id, 6)
            for n in range(NTC // 2):
                act.wait_ge(s_vp, n + 1)
                nc.scalar.activation(vones[:, 2 * n:2 * n + 2, :, :, 0],
                                     ring[SETUP_BANKS["values", n]][:, :].rearrange("p (i h d) -> p i h d", i=2, d=DH),
                                     ACT.Relu).then_inc(s_vr, 1)
            act.wait_ge(s_wq, 32)
            act.wait_ge(s_ks, NA)
            for kind, a, i, src in ring_order(AHEAD):
                take_job(-1, 1, True, kind, a, i, src)

            def half_step(b, hh, att, last, ahead):
                steps = ring_jobs(ahead)
                for i in range(UNITS):
                    if att:
                        exponentials(*att, i)
                    if b is not None:
                        for kind, a, k, src in steps[i]:
                            take_job(b, hh, ahead, kind, a, k, src)
                    if last and i == GROUP - 1:
                        take(*last, 3)
                    if att and i % (4 * GROUP) == GROUP - 1 and i > GROUP:
                        take(*att, i // (4 * GROUP) - 1)

            run(act, half_step)

        @block.vector
        def _(dve):
            def reduce_bank(b, hh, n, src):
                h, st, th = n // (NST * NTH), n // NTH % NST, n % NTH
                dve.wait_ge(s_mm, b * 2 * TILES + hh * TILES + n + 1)
                nc.vector.tensor_reduce(mx[:, st, h, th:th + 1], ring[src][:, :], AX.X, ALU.max).then_inc(s_mx, 1)

            def split_maxima(b, hh):
                step = b * 8 + hh * 4
                dve.wait_ge(s_mx, b * 2 * TILES + (hh + 1) * TILES)
                nc.vector.tensor_reduce(mneg[:, :, :], mx[:, :, :, :], AX.X, ALU.max, negate=True).then_inc(s_mc, 1)
                wait(dve, s_mT, b * 2 + hh)
                dve.wait_ge(s_mc, step + 1)
                nc.vector.tensor_copy(mparts[:, :, 0, :], mneg[:, :, :]).then_inc(s_mc, 1)
                dve.wait_ge(s_mc, step + 2)
                nc.vector.tensor_tensor(mrest[:, :, :], mneg[:, :, :], mparts[:, :, 0, :], ALU.subtract).then_inc(s_mc, 1)
                dve.wait_ge(s_mc, step + 3)
                nc.vector.tensor_copy(mparts[:, :, 1, :], mrest[:, :, :]).then_inc(s_mc, 1)
                dve.wait_ge(s_mc, step + 4)
                nc.vector.tensor_tensor(mparts[:, :, 2, :], mrest[:, :, :], mparts[:, :, 1, :],
                                        ALU.subtract).then_inc(s_ms, 1)

            def statistics(b, a):
                if a == 0:
                    dve.wait_ge(s_xin, (b + 1) * 16 + 16)
                for j in range(J):
                    nc.vector.bn_stats(stats[:, a, j, :], xin[:, a, j, :]).then_inc(s_stats, 1)

            def aggregate(b, a):
                for j in range(J):
                    nc.vector.bn_aggr(meanvar[:, a, j, :], stats[:, a, j, :]).then_inc(s_mv, 1)

            def normalise(b, a):
                if a == 0:
                    wait(dve, s_base, (b + 1) * NA)
                dve.wait_ge(s_rstd, (b + 1) * NA + a + 1)
                for j in range(J):
                    ins = nc.vector.tensor_scalar(xn[:, a, j, :], xin[:, a, j, :], rstd[:, a, j:j + 1],
                                                  shift[:, a, j:j + 1], ALU.mult, ALU.add)
                ins.then_inc(s_xn, 1)

            def clip(b, a, i, src):
                if a == 0 and i == 0:
                    wait(dve, s_badd, (b + 1) * 4)
                dve.wait_ge(s_f, (b + 1) * 4 + a * 2 + i + 1)
                nc.vector.tensor_scalar(dense[:, a, i, :], ring[src][:, :], LIMIT, -LIMIT,
                                        ALU.min, ALU.max).then_inc(s_dense, 1)

            def reciprocals(b, hh, i):
                if i == 0:
                    for r in range(2):
                        dve.wait_ge(s_gather[r], (b * 4 + hh * 2 + 2) * 16)
                part = fin[:, 1, i * P:(i + 1) * P]
                nc.vector.reciprocal(part, part).then_inc(s_rec, 1)

            nc.vector.memset(kstack[KS:KM, :, :], 1.0).then_inc(s_ones, 1)
            dve.wait_ge(s_wf, 48)
            nc.vector.tensor_scalar(sign_sb, wft_sb, 0.0, 2.0, ALU.is_ge, ALU.mult).then_inc(s_sg, 1)
            dve.wait_ge(s_sg, 1)
            nc.vector.tensor_scalar(sign_sb, sign_sb, 1.0, None, ALU.subtract).then_inc(s_sg, 1)
            dve.wait_ge(s_sg, 2)
            dve.wait_ge(s_sc, 1)
            scale_ps = ring[SETUP_BANKS["scale", 0]][:, 0:H]
            for ic in range(IC):
                ins = nc.vector.tensor_tensor(wf_sb[:, ic, :], scale_ps, sign_sb[:, ic, :], ALU.mult)
            ins.then_inc(s_ws, 1)
            for a in range(NA):
                statistics(-1, a)
            dve.wait_ge(s_stats, 8)
            for a in range(NA):
                aggregate(-1, a)
            for a in range(NA):
                normalise(-1, a)
            for kind, a, i, src in ring_order(AHEAD):
                if kind == "dense":
                    clip(-1, a, i, src)

            def half_step(b, hh, att, last, ahead):
                steps = ring_jobs(ahead)
                for i in range(UNITS):
                    q, u = i // GROUP, i % GROUP
                    if ahead and u == 0 and q < 2:
                        statistics(b, q)
                    if ahead and u == 0 and q in (1, 2):
                        dve.wait_ge(s_stats, (b + 1) * 8 + 4 * q)
                    if b is not None:
                        for kind, a, k, src in steps[i]:
                            if kind == "max":
                                reduce_bank(b, hh, a, src)
                            if kind == "dense":
                                clip(b, a, k, src)
                    if ahead and u == 0 and q in (1, 2):
                        aggregate(b, q - 1)
                    if ahead and u == 3 and q in (2, 3):
                        normalise(b, q - 2)
                    if last and 3 <= q < 7 and u % 2:
                        reciprocals(*last, 2 * (q - 3) + u // 2)
                    if b is not None and q == 12 and u == 3:
                        split_maxima(b, hh)

            run(dve, half_step)

        @block.gpsimd
        def _(pool):
            def tt(dst, in0, in1, op):
                return nc.gpsimd.tensor_tensor(dst, in0, in1, op)

            def split(dst, src, one, s, before):
                tt(dst[0], src, one, ALU.mult).then_inc(s, 1)
                pool.wait_ge(s, before + 1)
                tt(src, src, dst[0], ALU.subtract).then_inc(s, 1)
                pool.wait_ge(s, before + 2)
                tt(dst[1], src, one, ALU.mult).then_inc(s, 1)
                pool.wait_ge(s, before + 3)
                return tt(dst[2], src, dst[1], ALU.subtract)

            ones_block = C_ONE.broadcast_to([P, 2 * BANK]).rearrange("p (o s) -> p o s", o=2)

            def parts_of(a):
                return [parts[:, k, :, a * BANK:(a + 1) * BANK] for k in range(3)]

            def root(b, a):
                step = (b + 1) * 16 + a * 8
                small = [c.broadcast_to([P, J]) for c in (C_EPS, C_MHALF, C_3HALF, C_MONE)]
                eps, mhalf, threehalf, mone = small
                r, m = rstd[:, a, :], shift[:, a, :]
                pool.wait_ge(s_mv, (b + 1) * 8 + 4 * a + 4)
                tt(varp[:, :], meanvar[:, a, :, 1], eps, ALU.add).then_inc(s_rc, 1)
                pool.wait_ge(s_rc, step + 1)
                tt(r, varp[:, :], mhalf, ALU.pow).then_inc(s_rc, 1)
                pool.wait_ge(s_rc, step + 2)
                tt(newton[:, :], r, r, ALU.mult).then_inc(s_rc, 1)
                pool.wait_ge(s_rc, step + 3)
                tt(newton[:, :], newton[:, :], varp[:, :], ALU.mult).then_inc(s_rc, 1)
                pool.wait_ge(s_rc, step + 4)
                tt(newton[:, :], newton[:, :], mhalf, ALU.mult).then_inc(s_rc, 1)
                pool.wait_ge(s_rc, step + 5)
                tt(newton[:, :], newton[:, :], threehalf, ALU.add).then_inc(s_rc, 1)
                pool.wait_ge(s_rc, step + 6)
                tt(r, r, newton[:, :], ALU.mult).then_inc(s_rc, 1)
                pool.wait_ge(s_rc, step + 7)
                tt(m, meanvar[:, a, :, 0], mone, ALU.mult).then_inc(s_rc, 1)
                pool.wait_ge(s_rc, step + 8)
                tt(m, m, r, ALU.mult).then_inc(s_rstd, 1)

            def split_queries(b, a):
                if a == 0:
                    for hh in range(2):
                        for g in range(2):
                            wait(pool, s_load[hh][g], (b + 1) * 16 * len(TERMS))
                pool.wait_ge(s_qr, (b + 1) * 4 + a * 2 + 2)
                split(parts_of(a), proj[:, :, :], ones_block, s_qc, (b + 1) * 6 + a * 3).then_inc(s_split, 1)

            def base(b):
                wait(pool, s_bcopy, (b + 1) * 16)
                for a in range(NA):
                    pool.wait_ge(s_xn, (b + 1) * NA + a + 1)
                    tt(base_new[:, a, :], xin[:, a, :, :].rearrange("p j c -> p (j c)"),
                       xn[:, a, :, :].rearrange("p j c -> p (j c)"), ALU.add).then_inc(s_base, 1)
                for a in range(NA):
                    for i in range(2):
                        if i == 0:
                            pool.wait_ge(s_base, (b + 1) * NA + a + 1)
                        pool.wait_ge(s_dense, (b + 1) * 4 + a * 2 + i + 1)
                        part = base_new[:, a, i * BANK:(i + 1) * BANK]
                        tt(part, part, dense[:, a, i, :], ALU.add).then_inc(s_badd, 1)

            def finish(b, hh):
                pool.wait_ge(s_rec, b * 16 + hh * 8 + 8)
                tt(fin[:, 0, :], fin[:, 0, :], fin[:, 1, :], ALU.mult).then_inc(s_norm, 1)
                pool.wait_ge(s_norm, b * 2 + hh + 1)
                pool.wait_ge(s_bcopy, b * 16 + 16)
                tt(fin[:, 1, :].rearrange("p (a q j) -> p a q j", a=NA, j=J),
                   base_cur[:, hh, :].rearrange("p (a q j) -> p a q j", a=NA, j=J),
                   fin[:, 0, :].rearrange("p (a j q) -> p a q j", a=NA, j=J), ALU.add).then_inc(s_res, 1)

            for i, value in enumerate((EPS, -0.5, 1.5, -1.0, 1.0)):
                ins = nc.gpsimd.memset(const[:, i:i + 1], value)
            ins.then_inc(s_id, 1)
            nc.gpsimd.memset(ident[:, :], 0.0).then_inc(s_id, 1)
            nc.gpsimd.memset(identb[:, :], 0.0).then_inc(s_id, 1)
            nc.gpsimd.memset(vones[:, :, :, :, 1], 1.0).then_inc(s_id, 1)
            pool.wait_ge(s_id, 4)
            for m in (ident, identb):
                nc.gpsimd.affine_select(out=m[:, :], in_=m[:, :], compare_op=ALU.not_equal, fill=1.0, base=0,
                                        pattern=[[-1, P]], channel_multiplier=1).then_inc(s_id, 1)
            for a in range(NA):
                root(-1, a)
            for a in range(NTH):
                pool.wait_ge(s_kr, 2 * a + 2)
                split(parts_of(a), proj[:, :, :], ones_block, s_kc, 3 * a).then_inc(s_ks, 1)
            pool.wait_ge(s_kd, 4 * 16 * len(TERMS))
            for a in range(NA):
                split_queries(-1, a)
            base(-1)

            def half_step(b, hh, att, last, ahead):
                if ahead:
                    root(b, 0)
                    root(b, 1)
                    split_queries(b, 0)
                    split_queries(b, 1)
                if last:
                    finish(*last)
                if ahead:
                    base(b)

            run(pool, half_step)


def kernel(**inputs):
    import numpy as np
    import concourse.bacc as bacc
    from concourse.bass_utils import run_bass_kernel_spmd as run

    def head_order(a):
        return a.reshape(4, 4, 16, *a.shape[1:]).swapaxes(1, 2).reshape(a.shape)

    g = {k.removeprefix("L0_"): np.asarray(v) for k, v in inputs.items()}
    arrays = {
        "x": g["attn_queries"],
        "keys_t": g["attn_keys"][0].T,
        "values_t": g["attn_values"][0].T,
        "wq_t": head_order(g["attn_Wq_w"]).T,
        "bq": head_order(g["attn_Wq_b"]).reshape(2, 128).T,
        "wk_t": head_order(g["attn_Wk_w"]).T,
        "bk": head_order(g["attn_Wk_b"]).reshape(2, 128).T,
        "wv_t": g["attn_Wv_w"].T,
        "bv": g["attn_Wv_b"].reshape(1, 256),
        "wf_t": g["ffn_weights"].T,
        "scale": g["ffn_scale"].reshape(1, 256),
        "bias": g["ffn_bias"].reshape(1, 256),
    }
    arrays = {k: np.ascontiguousarray(v) for k, v in arrays.items()}
    nc = bacc.Bacc("TRN2", target_bir_lowering=False, num_devices=1)
    args = [nc.dram_tensor(k, v.shape, mybir.dt.from_np(v.dtype), kind="ExternalInput").ap() for k, v in arrays.items()]
    out = nc.dram_tensor("out", g["attn_queries"].shape, FP32, kind="ExternalOutput").ap()
    attention_block(nc, *args, out)
    return run(nc, [arrays], core_ids=[0]).results[0]["out"]
```

```python
from contextlib import ExitStack

import concourse.bass as bass
from concourse import mybir

FP32 = mybir.dt.float32
BF16 = mybir.dt.bfloat16
ALU = mybir.AluOpType
ACT = mybir.ActivationFunctionType
AX = mybir.AxisListType


def attention_block(nc: bass.Bass, x, keys_t, values_t, wq_t, bq, wk_t, bk, wv_t, bv, wf_t, scale, bias, out):
    P = 128
    NB, S, H = x.shape
    T = keys_t.shape[1]
    NH = 16
    DH = H // NH
    EPS = 1e-5
    LIMIT = 100.0
    BANK = 512
    IC = H // P
    HALF = NH // 2
    GROUP = 4
    J = H * 4 // S * 4
    NST = S // P
    NTH = T // BANK
    NTC = T // P
    NA = S // BANK
    TERMS = (0, 0, 1, 0, 2, 1)
    KTERMS = (0, 1, 0, 2, 0, 1)
    KS = len(TERMS) * DH
    KM = KS + 3
    QUADS = HALF // GROUP * NA * (NTC // 2)
    UNITS = QUADS * GROUP
    TILES = HALF * NST * NTH
    EXP_SCALE = float(DH) ** -0.5

    ctx = ExitStack()
    with ctx:
        def sb(name, shape, dt):
            return ctx.enter_context(nc.sbuf_tensor(name, shape, dt))

        def sem(name):
            return ctx.enter_context(nc.semaphore(name))

        recip_dram = nc.dram_tensor("recip", (HALF, S), FP32, kind="Internal").ap()

        kstack = sb("kstack", [KM, NH, T], BF16)
        qstack = [sb(f"qstack{i}", [KM, HALF, S], BF16) for i in range(2)]
        vones = sb("vones", [P, NTC, NH, DH, 2], FP32)
        probs = sb("probs", [P, 2 * GROUP, 2 * BANK], FP32)
        parts = sb("parts", [P, 3, 2, S], BF16)
        proj = sb("proj", [P, 2, BANK], FP32)
        mrows = proj[0:3 * HALF, 0, :].bitcast(BF16)
        xin = sb("xin", [P, NA, J, H], FP32)
        xn = sb("xn", [P, NA, J, H], FP32)
        xnT = sb("xnT", [P, IC, BANK], FP32)
        dense = sb("dense", [P, NA, 2, BANK], FP32)
        base_new = sb("base_new", [P, NA, J * H], FP32)
        base_cur = sb("base_cur", [P, NA, J * H], FP32)
        taken = sb("taken", [P, 2, BANK], FP32)
        fin = sb("fin", [P, 2, S], FP32)
        wq_sb = sb("wq_sb", [P, IC, H], FP32)
        wf_sb = sb("wf_sb", [P, IC, H], FP32)
        bias_parts = sb("bias_parts", [KM, H], BF16)
        sums = sb("sums", [HALF * S // P, P], FP32)
        ident = sb("ident", [P, P], FP32)
        identb = sb("identb", [P, P], BF16)
        mx = sb("mx", [P, NST, HALF, NTH], FP32)
        mneg = sb("mneg", [P, NST, HALF], FP32)
        mrest = sb("mrest", [P, NST, HALF], FP32)
        mparts = sb("mparts", [P, NST, 3, HALF], BF16)
        stats = sb("stats", [P, NA, J, 6], FP32)
        meanvar = sb("meanvar", [P, NA, J, 2], FP32)
        rstd = sb("rstd", [P, NA, J], FP32)
        shift = sb("shift", [P, NA, J], FP32)
        newton = sb("newton", [P, J], FP32)
        varp = sb("varp", [P, J], FP32)
        const = sb("const", [P, 5], FP32)
        bq_sb = sb("bq_sb", [P, 2], FP32)
        bk_sb = sb("bk_sb", [P, 2], FP32)
        C_EPS, C_MHALF, C_3HALF, C_MONE, C_ONE = (const[:, i:i + 1] for i in range(5))
        ones_row = vones[0:1, 0, 0:HALF, :, 1]

        keys_sb = probs[:, 0:2, :]
        vals_sb = probs[:, 2:4, :]
        wk_sb = probs[:, 4, 0:BANK].rearrange("p (c o) -> p c o", c=IC)
        wv_sb = probs[:, 4, BANK:2 * BANK].rearrange("p (c o) -> p c o", c=IC)
        wft_sb = probs[:, 5, 0:BANK].rearrange("p (c o) -> p c o", c=IC)
        sign_sb = probs[:, 5, BANK:2 * BANK].rearrange("p (c o) -> p c o", c=IC)
        key_proj = [dense[:, a, :, :] for a in range(NTH)]
        base_bf = base_cur[:, :, :].bitcast(BF16)
        key_parts = [base_bf[:, 0, :].rearrange("p (o t) -> p o t", o=2),
                     base_bf[:, 1, :].rearrange("p (o t) -> p o t", o=2),
                     fin[:, 0, :].bitcast(BF16).rearrange("p (o t) -> p o t", o=2)]
        scale_row = probs[0:1, 6, 0:H]
        bv_row = probs[0:1, 6, H:2 * H]
        bias_row = probs[0:1, 6, 2 * H:3 * H]
        bias_hml = probs[0:1, 7, 0:2 * H].bitcast(BF16).rearrange("o (k c) -> o k c", c=H)

        score_ps = [ctx.enter_context(nc.psum_tensor(f"score_ps{i}", [P, 2 * BANK], FP32)) for i in range(2)]
        value_ps = ctx.enter_context(nc.psum_tensor("value_ps", [P, BANK], FP32))
        RING = 3
        ring = [ctx.enter_context(nc.psum_tensor(f"ring{i}", [P, BANK], FP32)) for i in range(RING)]

        s_id = sem("s_id")
        s_ones = sem("s_ones")
        s_wk = sem("s_wk")
        s_wv = sem("s_wv")
        s_wf = sem("s_wf")
        s_wq = sem("s_wq")
        s_kp = sem("s_kp")
        s_kr = sem("s_kr")
        s_kc = sem("s_kc")
        s_ks = sem("s_ks")
        s_kd = sem("s_kd")
        s_vp = sem("s_vp")
        s_vr = sem("s_vr")
        s_sc = sem("s_sc")
        s_bs = sem("s_bs")
        s_bd = sem("s_bd")
        s_sg = sem("s_sg")
        s_ws = sem("s_ws")
        s_xin = sem("s_xin")
        s_stats = sem("s_stats")
        s_mv = sem("s_mv")
        s_rc = sem("s_rc")
        s_rstd = sem("s_rstd")
        s_xn = sem("s_xn")
        s_xT = sem("s_xT")
        s_xTc = sem("s_xTc")
        s_q = sem("s_q")
        s_qr = sem("s_qr")
        s_qc = sem("s_qc")
        s_split = sem("s_split")
        s_load = [[sem(f"s_load{i}{g}") for g in range(2)] for i in range(2)]
        s_f = sem("s_f")
        s_dense = sem("s_dense")
        s_base = sem("s_base")
        s_badd = sem("s_badd")
        s_bcopy = sem("s_bcopy")
        s_mm = sem("s_mm")
        s_mx = sem("s_mx")
        s_mc = sem("s_mc")
        s_ms = sem("s_ms")
        s_mT = sem("s_mT")
        s_mrow = sem("s_mrow")
        s_rows = [sem(f"s_rows{i}") for i in range(2)]
        s_scores = sem("s_scores")
        s_probs = sem("s_probs")
        s_pv = sem("s_pv")
        s_taken = sem("s_taken")
        s_pack = sem("s_pack")
        s_keep = sem("s_keep")
        s_spread = sem("s_spread")
        s_gather = [sem(f"s_gather{i}") for i in range(2)]
        s_rec = sem("s_rec")
        s_norm = sem("s_norm")
        s_res = sem("s_res")
        s_out = sem("s_out")

        def wait(eng, s, value):
            if not (isinstance(value, int) and value <= 0):
                eng.wait_ge(s, value)

        def quad_of(q):
            return q // (NA * NTC // 2), q // (NTC // 2) % NA, q % (NTC // 2)

        def ring_order(jobs, first):
            return [(*job, (first + n) % RING) for n, job in enumerate(jobs)]

        AHEAD = [(kind, a, i) for a in range(NA) for kind in ("turn", "project", "dense") for i in range(2)]
        AHEAD_UNITS = [18 + i * 3 for i in range(len(AHEAD))]
        AHEAD_TIME = {"turn": 0.25, "project": 0.95, "dense": 1.1}
        LEAD = 12
        ROWS_UNIT = 60
        KEY_JOBS = ring_order([(n // 2, n % 2) for n in range(2 * NTH)], 0)
        SCALE_BANK = len(KEY_JOBS) % RING
        FIRST_JOBS = ring_order(AHEAD, len(KEY_JOBS) + 1)
        VALUE_JOBS = ring_order([(n,) for n in range(NTC // 2)], len(KEY_JOBS) + 1 + len(AHEAD))
        assert (len(KEY_JOBS) + 1 + len(VALUE_JOBS)) % RING == 0 and len(AHEAD) % RING == 0 and LEAD % RING == 0

        def ring_jobs(ahead):
            weight = [1.0] * UNITS
            if ahead:
                weight[:20] = [0.75] * 20
                for job, i in zip(AHEAD, AHEAD_UNITS):
                    weight[i] += AHEAD_TIME[job[0]]
            steps, n, order = [], LEAD, 0
            for i in range(UNITS):
                upto = LEAD + round(TILES * sum(weight[:i + 1]) / sum(weight))
                jobs = [("max", k, 0) for k in range(n, upto)]
                n = upto
                if ahead:
                    jobs += [job for job, at in zip(AHEAD, AHEAD_UNITS) if at == i]
                if i == ROWS_UNIT:
                    jobs.append(("rows", 0, 0))
                steps.append([(*job, (order + k) % RING) for k, job in enumerate(jobs)])
                order += len(jobs)
            assert n == TILES + LEAD and order % RING == 0
            return steps

        LAST_BANK = [next(i for i, jobs in enumerate(ring_jobs(ahead)) if ("max", TILES - 1) in [j[:2] for j in jobs])
                     for ahead in (False, True)]
        assert max(LAST_BANK) < ROWS_UNIT

        def place(b, hh, n):
            if n >= TILES:
                if hh == 1 and isinstance(b, int) and b == NB - 1:
                    return None
                b, hh, n = (b, 1, n - TILES) if hh == 0 else (b + 1, 0, n - TILES)
            return b, hh, n // (NST * NTH), n // NTH % NST, n % NTH

        def run(eng, half_step):
            half_step(0, 0, None, None, False)
            half_step(0, 1, (0, 0), None, True)
            with eng.Fori(1, NB - 1) as b:
                half_step(b, 0, (b - 1, 1), (b - 1, 0), False)
                half_step(b, 1, (b, 0), (b - 1, 1), True)
            half_step(NB - 1, 0, (NB - 2, 1), (NB - 2, 0), False)
            half_step(NB - 1, 1, (NB - 1, 0), (NB - 2, 1), False)
            half_step(None, None, (NB - 1, 1), (NB - 1, 0), False)
            half_step(None, None, None, (NB - 1, 1), False)

        block = ctx.enter_context(nc.Block())

        @block.sync
        def _(sp):
            def load_x(b):
                sp.dma_start(xin[:, :, :, :], x[b].rearrange("(a p j) c -> p a j c", p=P, j=J)).then_inc(s_xin, 16)

            def stack(dst, head, src, g, terms, s):
                for r, term in enumerate(terms):
                    sp.dma_start(dst[r * DH:(r + 1) * DH, head:head + GROUP, :],
                                 src[term][g * GROUP * DH:(g + 1) * GROUP * DH, :]).then_inc(s, 16)

            def fixed(value):
                return value if isinstance(value, int) else sp.to_reg(value)

            def pack_sums(b, hh):
                first, second = fixed((b * 4 + hh * 2 + 2) * 16), fixed((b * 4 + hh * 2 + 2) * 16)
                sp.wait_ge(s_gather[0], first)
                sp.wait_ge(s_gather[1], second)
                sp.dma_start(sums[:, :], fin[0:P:DH, 1, :]).then_inc(s_pack, 16)

            def spread_reciprocals(b, hh):
                sp.wait_ge(s_rec, b * 2 + hh + 1)
                sp.dma_start(recip_dram.rearrange("h (c s) -> (h c) s", s=P), sums[:, :]).then_inc(s_keep, 16)
                sp.wait_ge(s_keep, (b * 2 + hh + 1) * 16)
                sp.dma_start(fin[:, 1, :], recip_dram.unsqueeze(1).broadcast_to([HALF, DH, S])).then_inc(s_spread, 16)

            def load_queries(b, hh, g):
                stack(qstack[hh], g * GROUP, [parts[:, k, hh, :] for k in range(3)], g, TERMS, s_load[hh][g])

            def gather(b, hh, a):
                before, now = fixed((b * 2 + hh) * 16), fixed(b * 8 + hh * 4 + a + 1)
                if a == 0:
                    wait(sp, s_out, before)
                sp.wait_ge(s_taken, now)
                g = a // NA
                sp.dma_start(fin[g * 64:(g + 1) * 64, :, (a % NA) * BANK:(a % NA + 1) * BANK],
                             taken[:, a % 2, :]).then_inc(s_gather[a % 2], 16)

            load_x(0)
            sp.dma_start(wk_sb, wk_t.rearrange("(c p) o -> p c o", p=P)).then_inc(s_wk, 16)
            sp.dma_start(bk_sb[:, :], bk).then_inc(s_wk, 16)
            sp.dma_start(keys_sb, keys_t.rearrange("(c p) t -> p c t", p=P)).then_inc(s_wk, 16)
            sp.dma_start(wft_sb, wf_t.rearrange("(c p) o -> p c o", p=P)).then_inc(s_wf, 16)
            sp.dma_start(scale_row, scale).then_inc(s_wf, 16)
            sp.dma_start(bias_row, bias).then_inc(s_wf, 16)
            sp.dma_start(wq_sb[:, :, :], wq_t.rearrange("(c p) o -> p c o", p=P)).then_inc(s_wq, 16)
            sp.dma_start(bq_sb[:, :], bq).then_inc(s_wq, 16)
            sp.dma_start(vals_sb, values_t.rearrange("(c p) t -> p c t", p=P)).then_inc(s_wv, 16)
            sp.dma_start(wv_sb, wv_t.rearrange("(c p) o -> p c o", p=P)).then_inc(s_wv, 16)
            sp.dma_start(bv_row, bv).then_inc(s_wv, 16)
            sp.wait_ge(s_bs, 4)
            sp.dma_start(bias_parts[KS:KM, :], bias_hml[:, 0:3, :]).then_inc(s_bd, 16)
            sp.wait_ge(s_ks, NA)
            for oc in range(2):
                for g in range(2):
                    stack(kstack, oc * HALF + g * GROUP, [part[:, oc, :] for part in key_parts], g, KTERMS, s_kd)
            sp.wait_ge(s_split, NA)
            load_queries(0, 0, 0)
            sp.wait_ge(s_kd, 4 * 16 * len(TERMS))

            def half_step(b, hh, att, last, ahead):
                if last:
                    gather(*last, 3)
                if b is not None:
                    load_queries(b, hh, 1)
                if last:
                    pack_sums(*last)
                if b is not None and hh == 0 and not (isinstance(b, int) and b == NB - 1):
                    sp.wait_ge(s_badd, b * 4 + 4)
                    load_x(b + 1)
                if last:
                    spread_reciprocals(*last)
                    fb, fh = last
                    result = out[fb].rearrange("(f p j) c -> f p (j c)", f=2, p=P)[fh]
                    sp.wait_ge(s_res, fb * 2 + fh + 1)
                    sp.dma_start(result, fin[:, 1, :]).then_inc(s_out, 16)
                if b is not None and hh == 1:
                    sp.wait_ge(s_badd, b * 4 + 4)
                    sp.dma_start(base_cur[:, :, :], base_new[:, :, :]).then_inc(s_bcopy, 16)
                if att:
                    gather(*att, 0)
                    gather(*att, 1)
                if b is not None and hh == 0:
                    load_queries(b, 1, 0)
                if ahead:
                    sp.wait_ge(s_split, b * NA + 2 * NA)
                    load_queries(b + 1, 0, 0)
                if att:
                    gather(*att, 2)
                if b is not None:
                    sp.wait_ge(s_mrow, b * 2 + hh + 1)
                    sp.dma_start(qstack[hh][KS:KM, :, :], mrows).then_inc(s_rows[hh], 16)

            run(sp, half_step)
            sp.wait_ge(s_out, NB * 2 * 16)

        @block.tensor
        def _(pe):
            users = []

            def bank(b, n, s, per, k, shift=0):
                if len(users) >= RING:
                    s0, per0, k0, shift0 = users[-RING]
                    pe.wait_ge(s0, (b + shift0) * per0 + k0)
                assert n == len(users) % RING
                users.append((s, per, k, shift))
                return ring[n]

            def scores(b, hh, u, c):
                g, a, tp = quad_of(u // GROUP)
                h = g * GROUP + u % GROUP
                if c == 0:
                    if u == 0:
                        if isinstance(b, int) and b == 0 and hh == 0:
                            pe.wait_ge(s_ones, 2)
                        pe.wait_ge(s_rows[hh], b * 16 + 16)
                    wait(pe, s_probs, b * 2 * UNITS + hh * UNITS + u - 1)
                tc = 2 * tp + c
                mm = pe.matmul(score_ps[u % 2][:, c * BANK:(c + 1) * BANK],
                               kstack[0:KM, hh * HALF + h, tc * P:(tc + 1) * P],
                               qstack[hh][0:KM, h, a * BANK:(a + 1) * BANK], start=True, stop=True)
                if c == 1:
                    mm.then_inc(s_scores, 1)

            def weigh(b, hh, q, c):
                g, a, tp = quad_of(q)
                if c == 0:
                    pe.wait_ge(s_probs, b * 2 * UNITS + hh * UNITS + GROUP * (q + 1))
                    if tp == 0:
                        wait(pe, s_taken, b * 8 + hh * 4 + q // 4)
                for h4 in range(GROUP):
                    mm = pe.matmul(value_ps[h4 * 32:(h4 + 1) * 32, :],
                                   vones[:, 2 * tp + c, hh * HALF + g * GROUP + h4, :, :],
                                   probs[:, q % 2 * GROUP + h4, c * BANK:(c + 1) * BANK],
                                   start=(tp == 0 and c == 0), stop=(tp == NTC // 2 - 1 and c == 1))
                if c == 1:
                    mm.then_inc(s_pv, 1)

            def maxima(b, hh, n, to):
                where = place(b, hh, n)
                if where is None:
                    assert to == len(users) % RING
                    users.append(users[-RING])
                    return
                nb, nh, h, st, th = where
                if n % (TILES // 2) == 0:
                    pe.wait_ge(s_load[nh][h // GROUP], nb * 16 * len(TERMS) + 16 * len(TERMS))
                ps = bank(b, to, s_mx, 2 * TILES, hh * TILES + n + 1)
                pe.matmul(ps[:, :], qstack[nh][0:KS, h, st * P:(st + 1) * P],
                          kstack[0:KS, nh * HALF + h, th * BANK:(th + 1) * BANK],
                          start=True, stop=True).then_inc(s_mm, 1)

            def turn_maxima(b, hh, to):
                ps = bank(b, to, s_mrow, 2, hh + 1)
                pe.wait_ge(s_ms, b * 2 + hh + 1)
                rows = ps[0:3 * HALF, :].bitcast(BF16)
                for st in range(NST):
                    mm = pe.transpose(rows[:, st * P:(st + 1) * P], mparts[:, st, :, :], identb[:, :])
                mm.then_inc(s_mT, 1)

            def next_batch(b, kind, a, i, to):
                if kind == "turn":
                    ps = bank(b, to, s_xTc, 4, a * 2 + i + 1, 1)
                    pe.wait_ge(s_xn, (b + 1) * NA + a + 1)
                    for j in range(J):
                        mm = pe.transpose(ps[:, j * P:(j + 1) * P], xn[:, a, j, i * P:(i + 1) * P], ident[:, :])
                    mm.then_inc(s_xT, 1)
                elif kind == "project":
                    ps = bank(b, to, s_qr, 4, a * 2 + i + 1, 1)
                    pe.wait_ge(s_xTc, (b + 1) * 4 + a * 2 + 2)
                    for ic in range(IC):
                        mm = pe.matmul(ps[:, :], wq_sb[:, ic, i * P:(i + 1) * P], xnT[:, ic, :],
                                       start=(ic == 0), stop=(ic == IC - 1))
                    mm.then_inc(s_q, 1)
                else:
                    ps = bank(b, to, s_dense, 4, a * 2 + i + 1, 1)
                    for j in range(2):
                        dst = ps[:, j * H:(j + 1) * H]
                        pe.matmul(dst, kstack[KS:KM, 0, 0:P], bias_parts[KS:KM, :], start=True, stop=False)
                        for ic in range(IC):
                            col = (i * 2 + j) * P
                            mm = pe.matmul(dst, xnT[:, ic, col:col + P], wf_sb[:, ic, :],
                                           start=False, stop=(ic == IC - 1))
                    mm.then_inc(s_f, 1)

            pe.wait_ge(s_wk, 48)
            for n, (a, oc, to) in enumerate(KEY_JOBS):
                ps = bank(-1, to, s_kr, 0, n + 1)
                for ic in range(IC):
                    mm = pe.matmul(ps[:, :], wk_sb[:, ic, oc * P:(oc + 1) * P],
                                   keys_sb[:, ic, a * BANK:(a + 1) * BANK],
                                   start=(ic == 0), stop=(ic == IC - 1))
                mm.then_inc(s_kp, 1)
            pe.wait_ge(s_id, 6)
            pe.wait_ge(s_wf, 48)
            ps = bank(-1, SCALE_BANK, s_ws, 0, 1)
            pe.matmul(ps[:, 0:H], ones_row, scale_row, start=True, stop=True).then_inc(s_sc, 1)
            pe.wait_ge(s_wq, 32)
            for job in FIRST_JOBS:
                if job[:3] == ("dense", 0, 0):
                    pe.wait_ge(s_bd, 16)
                    pe.wait_ge(s_ones, 1)
                    pe.wait_ge(s_ws, 1)
                next_batch(-1, *job)
            pe.wait_ge(s_wv, 48)
            for n, to in VALUE_JOBS:
                ps = bank(-1, to, s_vr, 0, n + 1)
                for i in range(2):
                    tc = 2 * n + i
                    dst = ps[:, i * H:(i + 1) * H]
                    pe.matmul(dst, ones_row, bv_row, start=True, stop=False)
                    for ic in range(IC):
                        mm = pe.matmul(dst, vals_sb[:, ic, tc * P:(tc + 1) * P], wv_sb[:, ic, :],
                                       start=False, stop=(ic == IC - 1))
                mm.then_inc(s_vp, 1)
            pe.wait_ge(s_kd, 4 * 16 * len(TERMS))
            for n in range(LEAD):
                maxima(-1, 1, TILES + n, n % RING)

            def half_step(b, hh, att, last, ahead):
                if b is not None and hh == 0:
                    users[-RING:] = [(s, per, k, shift - 1) for s, per, k, shift in users[-RING:]]
                steps = ring_jobs(ahead)
                for i in range(UNITS):
                    q, u = i // GROUP, i % GROUP
                    jobs = steps[i] if b is not None else []

                    def ring_work(some):
                        for kind, a, k, to in some:
                            if kind == "max":
                                maxima(b, hh, a, to)
                            elif kind == "rows":
                                turn_maxima(b, hh, to)
                            else:
                                next_batch(b, kind, a, k, to)

                    if att:
                        scores(*att, i, 0)
                    ring_work(jobs[0:1])
                    if att:
                        scores(*att, i, 1)
                    ring_work(jobs[1:2])
                    if u % 2 and (last if q == 0 else att):
                        weigh(*(last if q == 0 else att), (q - 1) % QUADS, u // 2)
                    ring_work(jobs[2:])

            run(pe, half_step)

        @block.scalar
        def _(act):
            def exponentials(b, hh, u):
                q = u // GROUP
                if u % GROUP == 0:
                    wait(act, s_pv, b * 2 * QUADS + hh * QUADS + q - 1)
                act.wait_ge(s_scores, b * 2 * UNITS + hh * UNITS + u + 1)
                nc.scalar.activation(probs[:, q % 2 * GROUP + u % GROUP, :], score_ps[u % 2][:, :],
                                     ACT.Exp, scale=EXP_SCALE).then_inc(s_probs, 1)

            def take(b, hh, a):
                wait(act, s_gather[a % 2], (b * 4 + hh * 2 + a // 2) * 16)
                act.wait_ge(s_pv, b * 2 * QUADS + hh * QUADS + 4 * a + 4)
                nc.scalar.activation(taken[:, a % 2, :], value_ps[:, :], ACT.Copy).then_inc(s_taken, 1)

            def take_job(b, hh, ahead, kind, a, i, src):
                if kind == "turn":
                    if i == 0:
                        wait(act, s_f, (b + 1) * 4 + a * 2)
                    act.wait_ge(s_xT, (b + 1) * 4 + a * 2 + i + 1)
                    nc.scalar.activation(xnT[:, i, :], ring[src][:, :], ACT.Copy).then_inc(s_xTc, 1)
                if kind == "project":
                    if i == 0:
                        wait(act, s_split, (b + 1) * NA + a)
                        if a == 0:
                            wait(act, s_rows[0], (b + 1) * 16)
                            wait(act, s_rows[1], b * 16)
                    act.wait_ge(s_q, (b + 1) * 4 + a * 2 + i + 1)
                    nc.scalar.activation(proj[:, i, :], ring[src][:, :], ACT.Relu,
                                         bias=bq_sb[:, i:i + 1]).then_inc(s_qr, 1)
                if kind == "rows":
                    act.wait_ge(s_mT, b * 2 + hh + 1)
                    wait(act, s_split, (b + 2 if ahead else b + 1) * NA)
                    wait(act, s_rows[1 - hh], (b + hh) * 16)
                    nc.scalar.activation(mrows, ring[src][0:3 * HALF, :].bitcast(BF16),
                                         ACT.Copy).then_inc(s_mrow, 1)

            act.wait_ge(s_wk, 48)
            for n, (a, oc, src) in enumerate(KEY_JOBS):
                act.wait_ge(s_kp, n + 1)
                nc.scalar.activation(key_proj[a][:, oc, :], ring[src][:, :], ACT.Relu,
                                     bias=bk_sb[:, oc:oc + 1]).then_inc(s_kr, 1)
            act.wait_ge(s_wq, 32)
            for kind, a, i, src in FIRST_JOBS:
                take_job(-1, 1, True, kind, a, i, src)
            act.wait_ge(s_id, 6)
            for n, src in VALUE_JOBS:
                act.wait_ge(s_vp, n + 1)
                nc.scalar.activation(vones[:, 2 * n:2 * n + 2, :, :, 0],
                                     ring[src][:, :].rearrange("p (i h d) -> p i h d", i=2, d=DH),
                                     ACT.Relu).then_inc(s_vr, 1)

            def half_step(b, hh, att, last, ahead):
                steps = ring_jobs(ahead)
                for i in range(UNITS):
                    if att:
                        exponentials(*att, i)
                    if b is not None:
                        for kind, a, k, src in steps[i]:
                            take_job(b, hh, ahead, kind, a, k, src)
                    if last and i == GROUP - 1:
                        take(*last, 3)
                    if att and i % (4 * GROUP) == GROUP - 1 and i > GROUP:
                        take(*att, i // (4 * GROUP) - 1)

            run(act, half_step)

        @block.vector
        def _(dve):
            def reduce_bank(b, hh, n, src):
                where = place(b, hh, n)
                if where is None:
                    return
                h, st, th = where[2:]
                dve.wait_ge(s_mm, b * 2 * TILES + hh * TILES + n + 1)
                nc.vector.tensor_reduce(mx[:, st, h, th:th + 1], ring[src][:, :], AX.X, ALU.max).then_inc(s_mx, 1)

            def split_maxima(b, hh):
                step = b * 8 + hh * 4
                dve.wait_ge(s_mx, b * 2 * TILES + (hh + 1) * TILES)
                nc.vector.tensor_reduce(mneg[:, :, :], mx[:, :, :, :], AX.X, ALU.max, negate=True).then_inc(s_mc, 1)
                wait(dve, s_mT, b * 2 + hh)
                dve.wait_ge(s_mc, step + 1)
                nc.vector.tensor_copy(mparts[:, :, 0, :], mneg[:, :, :]).then_inc(s_mc, 1)
                dve.wait_ge(s_mc, step + 2)
                nc.vector.tensor_tensor(mrest[:, :, :], mneg[:, :, :], mparts[:, :, 0, :], ALU.subtract).then_inc(s_mc, 1)
                dve.wait_ge(s_mc, step + 3)
                nc.vector.tensor_copy(mparts[:, :, 1, :], mrest[:, :, :]).then_inc(s_mc, 1)
                dve.wait_ge(s_mc, step + 4)
                nc.vector.tensor_tensor(mparts[:, :, 2, :], mrest[:, :, :], mparts[:, :, 1, :],
                                        ALU.subtract).then_inc(s_ms, 1)

            def statistics(b, a, j):
                if (a, j) == (0, 0):
                    dve.wait_ge(s_xin, (b + 1) * 16 + 16)
                nc.vector.bn_stats(stats[:, a, j, :], xin[:, a, j, :]).then_inc(s_stats, 1)

            def aggregate(a, j):
                nc.vector.bn_aggr(meanvar[:, a, j, :], stats[:, a, j, :]).then_inc(s_mv, 1)

            def normalise(b, a, j):
                if (a, j) == (0, 0):
                    wait(dve, s_base, (b + 1) * NA)
                if j == 0:
                    dve.wait_ge(s_rstd, (b + 1) * NA + a + 1)
                ins = nc.vector.tensor_scalar(xn[:, a, j, :], xin[:, a, j, :], rstd[:, a, j:j + 1],
                                              shift[:, a, j:j + 1], ALU.mult, ALU.add)
                if j == J - 1:
                    ins.then_inc(s_xn, 1)

            def clip(b, a, i, src):
                if a == 0 and i == 0:
                    wait(dve, s_badd, (b + 1) * 4)
                dve.wait_ge(s_f, (b + 1) * 4 + a * 2 + i + 1)
                nc.vector.tensor_scalar(dense[:, a, i, :], ring[src][:, :], LIMIT, -LIMIT,
                                        ALU.min, ALU.max).then_inc(s_dense, 1)

            def reciprocals(b, hh):
                dve.wait_ge(s_pack, (b * 2 + hh + 1) * 16)
                nc.vector.reciprocal(sums[:, :], sums[:, :]).then_inc(s_rec, 1)

            def split_keys(a):
                hi, mid, lo = (part[:, :, a * BANK:(a + 1) * BANK] for part in key_parts)
                rest = key_proj[a]
                dve.wait_ge(s_kr, 2 * a + 2)
                nc.vector.tensor_copy(hi, rest).then_inc(s_kc, 1)
                dve.wait_ge(s_kc, 3 * a + 1)
                nc.vector.tensor_tensor(rest, rest, hi, ALU.subtract).then_inc(s_kc, 1)
                dve.wait_ge(s_kc, 3 * a + 2)
                nc.vector.tensor_copy(mid, rest).then_inc(s_kc, 1)
                dve.wait_ge(s_kc, 3 * a + 3)
                nc.vector.tensor_tensor(lo, rest, mid, ALU.subtract).then_inc(s_ks, 1)

            nc.vector.memset(kstack[KS:KM, 0, :], 1.0).then_inc(s_ones, 1)
            ROW_TILES = [(a, j) for a in range(NA) for j in range(J)]
            for a, j in ROW_TILES:
                statistics(-1, a, j)
            dve.wait_ge(s_stats, len(ROW_TILES))
            for a, j in ROW_TILES:
                aggregate(a, j)
            dve.wait_ge(s_wf, 48)
            nc.vector.tensor_scalar(sign_sb, wft_sb, 0.0, 2.0, ALU.is_ge, ALU.mult).then_inc(s_sg, 1)
            parts_bf = [bias_hml[:, k, :] for k in range(3)]
            nc.vector.tensor_copy(parts_bf[0], bias_row).then_inc(s_bs, 1)
            dve.wait_ge(s_bs, 1)
            nc.vector.tensor_tensor(bias_row, bias_row, parts_bf[0], ALU.subtract).then_inc(s_bs, 1)
            dve.wait_ge(s_bs, 2)
            nc.vector.tensor_copy(parts_bf[1], bias_row).then_inc(s_bs, 1)
            dve.wait_ge(s_bs, 3)
            nc.vector.tensor_tensor(parts_bf[2], bias_row, parts_bf[1], ALU.subtract).then_inc(s_bs, 1)
            dve.wait_ge(s_sg, 1)
            nc.vector.tensor_scalar(sign_sb, sign_sb, 1.0, None, ALU.subtract).then_inc(s_sg, 1)
            dve.wait_ge(s_sg, 2)
            for a, j in ROW_TILES:
                normalise(-1, a, j)
            dve.wait_ge(s_sc, 1)
            scale_ps = ring[SCALE_BANK][:, 0:H]
            for ic in range(IC):
                ins = nc.vector.tensor_tensor(wf_sb[:, ic, :], scale_ps, sign_sb[:, ic, :], ALU.mult)
            ins.then_inc(s_ws, 1)
            for a in range(NTH):
                split_keys(a)
            dve.wait_ge(s_ks, NTH)
            for kind, a, i, src in FIRST_JOBS:
                if kind == "dense":
                    clip(-1, a, i, src)
            for n in range(LEAD):
                reduce_bank(-1, 1, TILES + n, n % RING)

            def half_step(b, hh, att, last, ahead):
                steps = ring_jobs(ahead)
                for i in range(UNITS):
                    q, u = i // GROUP, i % GROUP
                    if ahead and i < 8:
                        statistics(b, *ROW_TILES[i])
                    if ahead and i in (5, 9):
                        dve.wait_ge(s_stats, (b + 1) * 8 + i - 1)
                    if b is not None:
                        for kind, a, k, src in steps[i]:
                            if kind == "max":
                                reduce_bank(b, hh, a, src)
                                if a == TILES - 1:
                                    split_maxima(b, hh)
                            if kind == "dense":
                                clip(b, a, k, src)
                    if ahead and 5 <= i < 13:
                        aggregate(*ROW_TILES[i - 5])
                    if ahead and 12 <= i < 20:
                        normalise(b, *ROW_TILES[i - 12])
                    if last and q == 2 and u == 1:
                        reciprocals(*last)

            run(dve, half_step)

        @block.gpsimd
        def _(pool):
            def tt(dst, in0, in1, op):
                return nc.gpsimd.tensor_tensor(dst, in0, in1, op)

            def split(dst, src, one, s, before):
                tt(dst[0], src, one, ALU.mult).then_inc(s, 1)
                pool.wait_ge(s, before + 1)
                tt(src, src, dst[0], ALU.subtract).then_inc(s, 1)
                pool.wait_ge(s, before + 2)
                tt(dst[1], src, one, ALU.mult).then_inc(s, 1)
                pool.wait_ge(s, before + 3)
                return tt(dst[2], src, dst[1], ALU.subtract)

            ones_block = C_ONE.broadcast_to([P, 2 * BANK]).rearrange("p (o s) -> p o s", o=2)

            def parts_of(a):
                return [parts[:, k, :, a * BANK:(a + 1) * BANK] for k in range(3)]

            def root(b, a):
                step = (b + 1) * 16 + a * 8
                small = [c.broadcast_to([P, J]) for c in (C_EPS, C_MHALF, C_3HALF, C_MONE)]
                eps, mhalf, threehalf, mone = small
                r, m = rstd[:, a, :], shift[:, a, :]
                pool.wait_ge(s_mv, (b + 1) * 8 + 4 * a + 4)
                tt(varp[:, :], meanvar[:, a, :, 1], eps, ALU.add).then_inc(s_rc, 1)
                pool.wait_ge(s_rc, step + 1)
                tt(r, varp[:, :], mhalf, ALU.pow).then_inc(s_rc, 1)
                pool.wait_ge(s_rc, step + 2)
                tt(newton[:, :], r, r, ALU.mult).then_inc(s_rc, 1)
                pool.wait_ge(s_rc, step + 3)
                tt(newton[:, :], newton[:, :], varp[:, :], ALU.mult).then_inc(s_rc, 1)
                pool.wait_ge(s_rc, step + 4)
                tt(newton[:, :], newton[:, :], mhalf, ALU.mult).then_inc(s_rc, 1)
                pool.wait_ge(s_rc, step + 5)
                tt(newton[:, :], newton[:, :], threehalf, ALU.add).then_inc(s_rc, 1)
                pool.wait_ge(s_rc, step + 6)
                tt(r, r, newton[:, :], ALU.mult).then_inc(s_rc, 1)
                pool.wait_ge(s_rc, step + 7)
                tt(m, meanvar[:, a, :, 0], mone, ALU.mult).then_inc(s_rc, 1)
                pool.wait_ge(s_rc, step + 8)
                tt(m, m, r, ALU.mult).then_inc(s_rstd, 1)

            def split_queries(b, a):
                if a == 0:
                    for hh in range(2):
                        for g in range(2):
                            wait(pool, s_load[hh][g], (b + 1) * 16 * len(TERMS))
                pool.wait_ge(s_qr, (b + 1) * 4 + a * 2 + 2)
                split(parts_of(a), proj[:, :, :], ones_block, s_qc, (b + 1) * 6 + a * 3).then_inc(s_split, 1)

            def base(b):
                wait(pool, s_bcopy, (b + 1) * 16)
                for a in range(NA):
                    pool.wait_ge(s_xn, (b + 1) * NA + a + 1)
                    tt(base_new[:, a, :], xin[:, a, :, :].rearrange("p j c -> p (j c)"),
                       xn[:, a, :, :].rearrange("p j c -> p (j c)"), ALU.add).then_inc(s_base, 1)
                for a in range(NA):
                    for i in range(2):
                        if i == 0:
                            pool.wait_ge(s_base, (b + 1) * NA + a + 1)
                        pool.wait_ge(s_dense, (b + 1) * 4 + a * 2 + i + 1)
                        part = base_new[:, a, i * BANK:(i + 1) * BANK]
                        tt(part, part, dense[:, a, i, :], ALU.add).then_inc(s_badd, 1)

            def finish(b, hh):
                pool.wait_ge(s_spread, (b * 2 + hh + 1) * 16)
                tt(fin[:, 0, :], fin[:, 0, :], fin[:, 1, :], ALU.mult).then_inc(s_norm, 1)
                pool.wait_ge(s_norm, b * 2 + hh + 1)
                pool.wait_ge(s_bcopy, b * 16 + 16)
                tt(fin[:, 1, :].rearrange("p (a q j) -> p a q j", a=NA, j=J),
                   base_cur[:, hh, :].rearrange("p (a q j) -> p a q j", a=NA, j=J),
                   fin[:, 0, :].rearrange("p (a j q) -> p a q j", a=NA, j=J), ALU.add).then_inc(s_res, 1)

            for i, value in enumerate((EPS, -0.5, 1.5, -1.0, 1.0)):
                ins = nc.gpsimd.memset(const[:, i:i + 1], value)
            ins.then_inc(s_id, 1)
            nc.gpsimd.memset(ident[:, :], 0.0).then_inc(s_id, 1)
            nc.gpsimd.memset(identb[:, :], 0.0).then_inc(s_id, 1)
            nc.gpsimd.memset(vones[:, :, :, :, 1], 1.0).then_inc(s_id, 1)
            pool.wait_ge(s_id, 4)
            for m in (ident, identb):
                nc.gpsimd.affine_select(out=m[:, :], in_=m[:, :], compare_op=ALU.not_equal, fill=1.0, base=0,
                                        pattern=[[-1, P]], channel_multiplier=1).then_inc(s_id, 1)
            for a in range(NA):
                root(-1, a)
            for a in range(NA):
                split_queries(-1, a)
            base(-1)
            pool.wait_ge(s_badd, 4)
            nc.gpsimd.memset(kstack[KS:KM, 1:, :], 1.0).then_inc(s_ones, 1)
            pool.wait_ge(s_ones, 2)

            def half_step(b, hh, att, last, ahead):
                if ahead:
                    root(b, 0)
                    root(b, 1)
                if last:
                    finish(*last)
                if ahead:
                    split_queries(b, 0)
                    split_queries(b, 1)
                    base(b)

            run(pool, half_step)


def kernel(**inputs):
    import numpy as np
    import concourse.bacc as bacc
    from concourse.bass_utils import run_bass_kernel_spmd as run

    def head_order(a):
        return a.reshape(4, 4, 16, *a.shape[1:]).swapaxes(1, 2).reshape(a.shape)

    g = {k.removeprefix("L0_"): np.asarray(v) for k, v in inputs.items()}
    arrays = {
        "x": g["attn_queries"],
        "keys_t": g["attn_keys"][0].T,
        "values_t": g["attn_values"][0].T,
        "wq_t": head_order(g["attn_Wq_w"]).T,
        "bq": head_order(g["attn_Wq_b"]).reshape(2, 128).T,
        "wk_t": head_order(g["attn_Wk_w"]).T,
        "bk": head_order(g["attn_Wk_b"]).reshape(2, 128).T,
        "wv_t": g["attn_Wv_w"].T,
        "bv": g["attn_Wv_b"].reshape(1, 256),
        "wf_t": g["ffn_weights"].T,
        "scale": g["ffn_scale"].reshape(1, 256),
        "bias": g["ffn_bias"].reshape(1, 256),
    }
    arrays = {k: np.ascontiguousarray(v) for k, v in arrays.items()}
    nc = bacc.Bacc("TRN2", target_bir_lowering=False, num_devices=1)
    args = [nc.dram_tensor(k, v.shape, mybir.dt.from_np(v.dtype), kind="ExternalInput").ap() for k, v in arrays.items()]
    out = nc.dram_tensor("out", g["attn_queries"].shape, FP32, kind="ExternalOutput").ap()
    attention_block(nc, *args, out)
    return run(nc, [arrays], core_ids=[0]).results[0]["out"]
```
